# Optimizing a Trainium2 kernel written in Bass

```python
import numpy as np
import jax
import jax.numpy as jnp

def _softmax(x, axis=-1):
    return jax.nn.softmax(x, axis=axis)
def _gelu(x):
    return jax.nn.gelu(x, approximate=True)
def _silu(x):
    return jax.nn.silu(x)
def _sigmoid(x):
    return jax.nn.sigmoid(x)
def _layernorm(x, axis=-1, eps=1e-5):
    m = jnp.mean(x, axis=axis, keepdims=True)
    v = jnp.var(x, axis=axis, keepdims=True)
    return (x - m) / jnp.sqrt(v + eps)
def _scatter_add(tgt, idx, src, axis=0):
    return tgt.at[idx].add(src)
def _segment_sum(src, seg, n):
    return jax.ops.segment_sum(src, seg, n)

kernel_name = 'mk_rec_standalone_d1_rec_c916c6'

def setup_inputs(seed: int = 0):
    np.random.seed(seed)
    _w = jnp.asarray
    def _rec_inputs():
        import jax
        import jax.numpy as jnp
        _rk = jax.random.key(seed)
        r_embedded_features = -0.000611745 + 1.00059 * jax.random.normal(jax.random.fold_in(_rk, 1), (1024, 39, 16), jnp.float32)
        return r_embedded_features
    r_embedded_features = _rec_inputs()
    def _L0_rec_setup():
        import jax, jax.numpy as jnp
        import numpy as np
        B, F0, D = (4096, 39, 16)
        CIN = [128, 128, 128]

        def _cin_layer(X0, Xi, W, b):
            H = W.shape[0]
            F0_, Fi = (X0.shape[1], Xi.shape[1])
            Wr = W.reshape(H, F0_, Fi)
            return jnp.einsum('hjk,bjd,bkd->bhd', Wr, X0, Xi) + b[None, :, None]
        key = jax.random.key(seed)
        ks = jax.random.split(key, 4)
        x = jax.random.normal(ks[0], (B, F0, D), dtype=jnp.float32)
        fields = [F0] + CIN
        inp = {'embedded_features': x}
        for i in range(len(CIN)):
            cin = F0 * fields[i]
            cout = fields[i + 1]
            kw = jax.random.fold_in(ks[1], i)
            inp[f'W{i}'] = jax.random.normal(kw, (cout, cin), dtype=jnp.float32) / np.sqrt(cin)
            inp[f'b{i}'] = jnp.zeros((cout,), dtype=jnp.float32)
        return inp
    _L0_rec_all = _L0_rec_setup()
    _L0_rec_in = {k: v for k, v in _L0_rec_all.items() if k in ('W0', 'b0', 'W1', 'b1', 'W2', 'b2', )}
    del _L0_rec_all

    return {
        "r_embedded_features": r_embedded_features,
        "L0_rec_W0": _L0_rec_in["W0"],
        "L0_rec_b0": _L0_rec_in["b0"],
        "L0_rec_W1": _L0_rec_in["W1"],
        "L0_rec_b1": _L0_rec_in["b1"],
        "L0_rec_W2": _L0_rec_in["W2"],
        "L0_rec_b2": _L0_rec_in["b2"],
    }

def reference(r_embedded_features, L0_rec_W0, L0_rec_b0, L0_rec_W1, L0_rec_b1, L0_rec_W2, L0_rec_b2):
    import jax
    import jax.numpy as jnp
    def _L0_rec_ref(embedded_features, W0, b0, W1, b1, W2, b2):
        import jax, jax.numpy as jnp
        import numpy as np
        B, F0, D = (4096, 39, 16)
        CIN = [128, 128, 128]

        def _cin_layer(X0, Xi, W, b):
            H = W.shape[0]
            F0_, Fi = (X0.shape[1], Xi.shape[1])
            Wr = W.reshape(H, F0_, Fi)
            return jnp.einsum('hjk,bjd,bkd->bhd', Wr, X0, Xi) + b[None, :, None]
        X0 = embedded_features
        Ws = [(W0, b0), (W1, b1), (W2, b2)]
        Xi = X0
        res = []
        for W, b in Ws:
            Xi = _cin_layer(X0, Xi, W, b)
            res.append(Xi.sum(axis=2))
        return jnp.concatenate(res, axis=1)

    y = _L0_rec_ref(r_embedded_features, L0_rec_W0, L0_rec_b0, L0_rec_W1, L0_rec_b1, L0_rec_W2, L0_rec_b2)
    return y


_drawn_inputs = setup_inputs


def setup_inputs(seed=0):
    import zlib

    import numpy as np

    out = dict(_drawn_inputs(seed))
    spreads = {'L0_rec_b0': (0.0, 0.1), 'L0_rec_b1': (0.0, 0.1), 'L0_rec_b2': (0.0, 0.1)}
    factors = {}
    for name, (base, spread) in spreads.items():
        noise = np.random.default_rng([zlib.crc32(name.encode()), seed]).standard_normal(out[name].shape)
        drawn = base * np.exp(spread * noise) if base else spread * noise
        out[name] = jnp.asarray(drawn.astype(out[name].dtype))
    for name, factor in factors.items():
        out[name] = (out[name] * factor).astype(out[name].dtype)
    return out
```

```python
from contextlib import ExitStack

import concourse.bass as bass
import numpy as np
from concourse import mybir

P = 128
BATCH, FIELDS, EMB = 1024, 39, 16
HID = 128
COLS = BATCH * EMB
TILE_B = P // EMB
MACRO = 512
TILES = MACRO // P
MACROS = COLS // MACRO
STEPS = MACROS // 2
STEP_B = 2 * TILES * TILE_B
COPIES = P // FIELDS
SHIFTS = (FIELDS + 1) // 2
GROUPS = -(-SHIFTS // COPIES)
LOW = 64
CJ = 4
CHUNKS = -(-FIELDS // CJ)
JX = FIELDS + 1
ACT_CHUNKS = (1, 3, 6, 8)
DVE_CHUNKS = tuple(c for c in range(CHUNKS) if c not in ACT_CHUNKS)
NA, ND = len(ACT_CHUNKS), len(DVE_CHUNKS)
MC = TILES * CHUNKS
BANKS = 4
SEL_AT = [3 + 9 * g // 2 for g in range(GROUPS)]
SUM_AT = [s + 4 for s in SEL_AT]
T_AT = 6
SAVE_AT = 8
R_AT = 3

F32 = mybir.dt.float32
F32R = mybir.dt.float32r
ALU = mybir.AluOpType
ACT = mybir.ActivationFunctionType
AX_X = mybir.AxisListType.X


def first_at(chunks, at):
    return min(t * CHUNKS + c for t in range(TILES) for c in chunks if t * CHUNKS + c >= at)


def cin_kernel(nc, x_sel, x_rep, x_row, spread, own, w0a, w0b, w1, w2, b0, b1, b2, out):
    with ExitStack() as ctx:
        def sb(name, shape, dt=F32):
            return ctx.enter_context(nc.sbuf_tensor(name, shape, dt))

        def psum(name, shape):
            return ctx.enter_context(nc.psum_tensor(name, shape, F32))

        def sem(name):
            return ctx.enter_context(nc.semaphore(name))

        y = [psum(f"y{b}", [P, CJ, HID]) for b in range(BANKS)]
        spread_ps = psum("spread_ps", [P, MACRO])
        x1_ps = psum("x1_ps", [P, MACRO])
        pair_ps = psum("pair_ps", [P, JX, TILE_B])
        r_ps = psum("r_ps", [P, STEP_B])

        w0_a = sb("w0_a", [P, GROUPS, HID])
        w0_b = sb("w0_b", [P, GROUPS, HID])
        w0_s = sb("w0_s", [P, GROUPS, HID])
        w1_f = sb("w1_f", [P, FIELDS, HID])
        w1_h = sb("w1_h", [P, FIELDS, HID], F32R)
        w1_l = sb("w1_l", [P, FIELDS, HID], F32R)
        w2_s = sb("w2_s", [P, FIELDS, HID])
        spread_f = sb("spread_f", [P, GROUPS, P])
        spread_r = sb("spread_r", [P, GROUPS, P], F32R)
        own_s = sb("own_s", [P, TILE_B])
        b0_s = sb("b0_s", [P, 1])
        b0_16 = sb("b0_16", [P, 1])
        b1_row = sb("b1_row", [P, HID])
        b2_s = sb("b2_s", [P, 1])
        b2_16 = sb("b2_16", [P, 1])

        xs_f = [sb(f"xs_f{p}", [P, MACRO]) for p in range(2)]
        xs_r = [sb(f"xs_r{p}", [P, MACRO], F32R) for p in range(2)]
        xs_l = sb("xs_l", [P, MACRO])
        xr = [sb(f"xr{p}", [P, MACRO]) for p in range(2)]
        xn = [sb(f"xn{p}", [P, TILES, JX]) for p in range(2)]
        z = [sb(f"z{p}", [P, MACRO]) for p in range(2)]
        x1_h = [sb(f"x1_h{p}", [P, MACRO], F32R) for p in range(2)]
        x1_l = [sb(f"x1_l{p}", [P, MACRO], F32R) for p in range(2)]

        acc_d = [sb(f"acc_d{p}", [P, CJ, HID]) for p in range(2)]
        acc_a = [sb(f"acc_a{p}", [P, CJ, HID]) for p in range(2)]
        prod = [sb(f"prod{p}", [P, CJ, HID]) for p in range(NA - 1)]
        x2 = [sb(f"x2_{p}", [P, HID]) for p in range(2)]
        diag = [sb(f"diag{p}", [P, JX, TILE_B]) for p in range(2)]
        pair = sb("pair", [P, JX, STEP_B])
        out0 = sb("out0", [P, BATCH + MACRO // EMB])
        out1 = sb("out1", [P, STEP_B + BATCH])
        out2 = sb("out2", [P, STEP_B + BATCH])

        s_consts = sem("s_consts")
        s_w1 = [sem(f"s_w1_{q}") for q in range(CHUNKS)]
        s_w2 = sem("s_w2")
        s_x = [sem(f"s_x{p}") for p in range(2)]
        s_xn = [sem(f"s_xn{p}") for p in range(2)]
        s_spread = sem("s_spread")
        s_w0 = sem("s_w0")
        s_w1h = sem("s_w1h")
        s_w1l = sem("s_w1l")
        s_zero = sem("s_zero")
        s_xhi = sem("s_xhi")
        s_xlo = sem("s_xlo")
        s_xs = sem("s_xs")
        s_sel = sem("s_sel")
        s_z = sem("s_z")
        s_sum0 = sem("s_sum0")
        s_x1h = sem("s_x1h")
        s_x1l = sem("s_x1l")
        s_out0 = sem("s_out0")
        s_y = [sem(f"s_y{b}") for b in range(BANKS)]
        s_dve = sem("s_dve")
        s_act = sem("s_act")
        s_chain = sem("s_chain")
        s_x2 = sem("s_x2")
        s_diag = sem("s_diag")
        s_pair = sem("s_pair")
        s_pair_sb = sem("s_pair_sb")
        s_r = sem("s_r")
        s_out1 = sem("s_out1")
        s_out2 = sem("s_out2")
        s_last = sem("s_last")
        s_store = sem("s_store")

        block = ctx.enter_context(nc.Block())
        CHAIN = NA + 1

        def dve_through(tile, c):
            return ND * (tile + 1) + DVE_CHUNKS.index(c) + 1

        def act_through(tile, c):
            return NA * (tile + 1) + ACT_CHUNKS.index(c) + 1

        @block.sync
        def _(sp):
            def load_x(g, par):
                sp.dma_start(xs_f[par][:, :], x_sel[:, bass.ds(g * MACRO, MACRO)]).then_inc(s_x[par], 16)
                sp.dma_start(xr[par][:, :], x_rep[:, bass.ds(g * MACRO, MACRO)]).then_inc(s_x[par], 16)

            def load_xn(g, par):
                sp.dma_start(xn[par][:, :, :].rearrange("p t j -> p (t j)"),
                             x_row[bass.ds(g * P, P), :]).then_inc(s_xn[par], 16)

            load_x(0, 0)
            for dst, src in ((spread_f[:, :, :], spread), (w0_a[:, :, :], w0a), (w0_b[:, :, :], w0b)):
                sp.dma_start(dst.rearrange("p g m -> p (g m)"), src).then_inc(s_consts, 16)
            sp.dma_start(own_s[:, :], own).then_inc(s_consts, 16)
            sp.dma_start(b0_s[:, :], b0.rearrange("(h o) -> h o", o=1)).then_inc(s_consts, 16)
            sp.dma_start(b2_s[:, :], b2.rearrange("(h o) -> h o", o=1)).then_inc(s_consts, 16)
            sp.dma_start(b1_row[:, :], b1.rearrange("(o h) -> o h", o=1).to_broadcast([P, HID])).then_inc(s_consts, 16)
            load_xn(0, 0)
            w1_v = w1.rearrange("k (j h) -> k j h", h=HID)
            for q in range(CHUNKS):
                js = slice(CJ * q, min(CJ * q + CJ, FIELDS))
                sp.dma_start(w1_f[:, js, :], w1_v[:, js, :]).then_inc(s_w1[q], 16)
            sp.dma_start(w2_s[:, :, :].rearrange("p j h -> p (j h)"), w2).then_inc(s_w2, 16)
            with sp.Fori(0, STEPS) as i:
                for a in range(2):
                    g, par = 2 * i + a + 1, (a + 1) % 2
                    sp.wait_ge(s_out0, g)
                    load_x(g, par)
                    sp.wait_ge(s_dve, TILES * ND * (g - 1) + ND)
                    sp.wait_ge(s_act, TILES * NA * (g - 1) + NA)
                    sp.wait_ge(s_diag, TILES * (g - 1) + 1)
                    load_xn(g, par)
            sp.wait_ge(s_last, 1)
            sp.dma_start(out[0], out0[:, 0:BATCH]).then_inc(s_store, 16)
            sp.wait_ge(s_out1, STEPS + 1)
            sp.dma_start(out[1], out1[:, STEP_B:]).then_inc(s_store, 16)
            sp.wait_ge(s_out2, STEPS + 2)
            sp.dma_start(out[2], out2[:, STEP_B:]).then_inc(s_store, 16)
            sp.wait_ge(s_store, 48)

        @block.tensor
        def _(pe):
            def spread_fields(g, par, t):
                if t == 0:
                    pe.wait_ge(s_xs, g + 1)
                pe.matmul(spread_ps[:, :], spread_r[:, t, :], xs_r[par][:, :],
                          start=True, stop=True).then_inc(s_sel, 1)

            def sum_products(g, par, t):
                pe.wait_ge(s_z, GROUPS * g + t + 1)
                if t == 0:
                    pe.wait_ge(s_out0, g + 1)
                last = pe.matmul(x1_ps[:, :], w0_s[:, t, :], z[t % 2][:, :],
                                 start=(t == 0), stop=(t == GROUPS - 1))
                if t == GROUPS - 1:
                    last.then_inc(s_sum0, 1)

            def layer1(i, a, t, c):
                q = (a * TILES + t) * CHUNKS + c
                bank = q % BANKS
                tile, before = 2 * TILES * i + (q - BANKS) // CHUNKS, (q - BANKS) % CHUNKS
                if before in ACT_CHUNKS:
                    pe.wait_ge(s_act, act_through(tile, before))
                else:
                    pe.wait_ge(s_dve, dve_through(tile, before))
                js = slice(CJ * c, min(CJ * c + CJ, FIELDS))
                n = js.stop - js.start
                hi = x1_h[a][:, t * P:t * P + P]
                lo = x1_l[a][:, t * P:t * P + P]
                pe.matmul(y[bank][:, 0:n, :], hi, w1_h[:, js, :], start=True, stop=False)
                pe.matmul(y[bank][:, 0:n, :], hi, w1_l[:, js, :], start=False, stop=False)
                pe.matmul(y[bank][:, 0:n, :], lo, w1_h[:, js, :], start=False, stop=True).then_inc(s_y[bank], 1)

            def pair_sums(tile, par):
                pe.wait_ge(s_x2, tile + 3)
                pe.wait_ge(s_diag, tile + 2)
                pe.wait_ge(s_pair_sb, tile + 2)
                pe.matmul(pair_ps[:, :, :], x2[par][:, :], diag[par][:, :, :],
                          start=True, stop=True).then_inc(s_pair, 1)

            def layer2(i):
                pe.wait_ge(s_pair_sb, 2 * TILES * i + 2)
                pe.wait_ge(s_out2, i + 1)
                for j in range(FIELDS):
                    last = pe.matmul(r_ps[:, :], w2_s[:, j, :], pair[:, j, :],
                                     start=(j == 0), stop=(j == FIELDS - 1))
                last.then_inc(s_r, 1)

            pe.wait_ge(s_spread, 1)
            pe.wait_ge(s_w0, 1)
            for t in range(GROUPS):
                spread_fields(0, 0, t)
                sum_products(0, 0, t)
            pe.wait_ge(s_w1h, CHUNKS)
            pe.wait_ge(s_w1l, CHUNKS)
            pe.wait_ge(s_w2, 16)
            pe.wait_ge(s_zero, 1)
            with pe.Fori(0, STEPS) as i:
                for a in range(2):
                    g = 2 * i + a + 1
                    pe.wait_ge(s_x1l, g)
                    for t in range(TILES):
                        for c in range(CHUNKS):
                            r = t * CHUNKS + c
                            if r in SUM_AT:
                                sum_products(g, 1 - a, SUM_AT.index(r))
                            if r in SEL_AT:
                                spread_fields(g, 1 - a, SEL_AT.index(r))
                            if c == T_AT:
                                u = a * TILES + t
                                pair_sums(2 * TILES * i + u - 1, (u + 1) % 2)
                            if (a, t, c) == (0, 1, R_AT):
                                layer2(i)
                            layer1(i, a, t, c)
            pair_sums(TILES * MACROS - 1, 1)
            layer2(STEPS)

        @block.scalar
        def _(act):
            def round_x(g, par, loads):
                act.wait_ge(s_x[par], loads)
                if not isinstance(g, int):
                    act.wait_ge(s_out0, g)
                act.activation(xs_r[par][:, :], xs_f[par][:, :], ACT.Copy).then_inc(s_xhi, 1)

            def place_low(g, par):
                act.wait_ge(s_xlo, g + 1)
                act.activation(xs_r[par][LOW:, :], xs_l[LOW:, :], ACT.Copy).then_inc(s_xs, 1)

            def round_x1(g, par):
                act.wait_ge(s_sum0, g + 1)
                act.activation(x1_h[par][:, :], x1_ps[:, :], ACT.Identity, bias=b0_s[:, 0:1]).then_inc(s_x1h, 1)

            def weigh(i, a, t, c):
                q = (a * TILES + t) * CHUNKS + c
                bank, use = q % BANKS, 2 * MC // BANKS * i + q // BANKS
                tile = 2 * TILES * i + a * TILES + t
                k = ACT_CHUNKS.index(c)
                if k == 0:
                    act.wait_ge(s_x2, tile + 1)
                    dst = acc_a[t % 2]
                else:
                    act.wait_ge(s_chain, CHAIN * tile + k)
                    dst = prod[k - 1]
                act.wait_ge(s_y[bank], use + 1)
                for s in range(CJ):
                    last = act.activation(dst[:, s, :], y[bank][:, s, :], ACT.Copy,
                                          scale=xn[a][:, t, CJ * c + s:CJ * c + s + 1])
                last.then_inc(s_act, 1)

            def save_pair(tile, u):
                act.wait_ge(s_pair, tile + 2)
                act.activation(pair[:, :, TILE_B * u:TILE_B * u + TILE_B], pair_ps[:, :, :],
                               ACT.Copy).then_inc(s_pair_sb, 1)

            act.wait_ge(s_consts, 7 * 16)
            act.activation(spread_r[:, :, :], spread_f[:, :, :], ACT.Copy).then_inc(s_spread, 1)
            act.activation(prod[-1][:, 0, 0:TILE_B], own_s[:, :], ACT.Copy).then_inc(s_act, NA)
            act.activation(prod[-1][:, 1, 0:TILE_B], own_s[:, :], ACT.Copy).then_inc(s_pair_sb, 1)
            round_x(0, 0, 32)
            place_low(0, 0)
            for q in range(CHUNKS):
                js = slice(CJ * q, min(CJ * q + CJ, FIELDS))
                act.wait_ge(s_w1[q], 16)
                act.activation(w1_h[:, js, :], w1_f[:, js, :], ACT.Copy).then_inc(s_w1h, 1)
                if q == CHUNKS // 2:
                    round_x1(0, 0)
            act.wait_ge(s_zero, 1)
            with act.Fori(0, STEPS) as i:
                for a in range(2):
                    g = 2 * i + a + 1
                    act.wait_ge(s_xn[a], 16 * i + 16)
                    round_x(g, 1 - a, 32 * (i + a) + 32)
                    for t in range(TILES):
                        for c in ACT_CHUNKS:
                            r = t * CHUNKS + c
                            if r == ACT_CHUNKS[1]:
                                place_low(g, 1 - a)
                            if r == first_at(ACT_CHUNKS, SUM_AT[-1] + 1):
                                round_x1(g, 1 - a)
                            if c == SAVE_AT:
                                u = a * TILES + t
                                if u == 1:
                                    act.wait_ge(s_out1, i + 1)
                                save_pair(2 * TILES * i + u - 1, (u - 1) % (2 * TILES))
                            weigh(i, a, t, c)
            save_pair(TILES * MACROS - 1, 2 * TILES - 1)

        @block.vector
        def _(dve):
            def product(g, par, t):
                dve.wait_ge(s_sel, GROUPS * g + t + 1)
                dve.tensor_tensor(z[t % 2][:, :], spread_ps[:, :], xr[par][:, :], ALU.mult).then_inc(s_z, 1)

            def low_x1(g, par):
                dve.wait_ge(s_x1h, g + 1)
                dve.scalar_tensor_tensor(out=x1_l[par][:, :], in0=x1_ps[:, :], scalar=b0_s[:, 0:1],
                                         in1=x1_h[par][:, :].bitcast(F32), op0=ALU.add,
                                         op1=ALU.subtract).then_inc(s_x1l, 1)

            def sum_x1(g):
                dve.tensor_reduce(out0[:, bass.ds(g * (MACRO // EMB), MACRO // EMB)],
                                  x1_ps[:, :].rearrange("h (b d) -> h b d", d=EMB), AX_X,
                                  ALU.add).then_inc(s_out0, 1)

            def weigh(i, a, t, c):
                q = (a * TILES + t) * CHUNKS + c
                bank, use = q % BANKS, 2 * MC // BANKS * i + q // BANKS
                tile = 2 * TILES * i + a * TILES + t
                k = DVE_CHUNKS.index(c)
                acc = acc_d[t % 2]
                if k == 0:
                    dve.wait_ge(s_x2, tile + 1)
                else:
                    dve.wait_ge(s_dve, ND * (tile + 1) + k)
                dve.wait_ge(s_y[bank], use + 1)
                n = min(CJ, FIELDS - CJ * c)
                for s in range(n):
                    x = xn[a][:, t, CJ * c + s:CJ * c + s + 1]
                    if k == 0 and s > 0:
                        last = dve.tensor_scalar(acc[:, s, :], y[bank][:, s, :], x, None, ALU.mult)
                    else:
                        last = dve.scalar_tensor_tensor(out=acc[:, s, :], in0=y[bank][:, s, :], scalar=x,
                                                        in1=acc[:, s, :] if k else b1_row[:, :],
                                                        op0=ALU.mult, op1=ALU.add)
                last.then_inc(s_dve, 1)

            def save_out(i):
                dve.wait_ge(s_pair_sb, 2 * TILES * i + 2)
                dve.tensor_scalar(out1[:, bass.ds(i * STEP_B, STEP_B)], pair[:, FIELDS, :], 1.0, None,
                                  ALU.mult).then_inc(s_out1, 1)

            def save_out2(i):
                dve.wait_ge(s_r, i + 1)
                dve.tensor_scalar(out2[:, bass.ds(i * STEP_B, STEP_B)], r_ps[:, :], b2_16[:, 0:1], None,
                                  ALU.add).then_inc(s_out2, 1)

            dve.memset(pair[:, :, :], 0.0).then_inc(s_zero, 1)
            dve.memset(acc_d[1][:, 0, 0:2], 0.0).then_inc(s_dve, ND)
            dve.wait_ge(s_consts, 7 * 16)
            dve.tensor_tensor(w0_s[:, :, :], w0_a[:, :, :], w0_b[:, :, :], ALU.add).then_inc(s_w0, 1)
            dve.tensor_scalar(b0_16[:, :], b0_s[:, :], float(EMB), None, ALU.mult).then_inc(s_out0, 1)
            dve.tensor_scalar(b2_16[:, :], b2_s[:, :], float(EMB), None, ALU.mult).then_inc(s_out2, 1)
            dve.wait_ge(s_x[0], 32)
            for t in range(GROUPS):
                product(0, 0, t)
            low = 0
            for q in range(CHUNKS):
                js = slice(CJ * q, min(CJ * q + CJ, FIELDS))
                dve.wait_ge(s_w1h, q + 1)
                dve.tensor_tensor(w1_l[:, js, :], w1_f[:, js, :], w1_h[:, js, :].bitcast(F32),
                                  ALU.subtract).then_inc(s_w1l, 1)
            low_x1(0, 0)
            sum_x1(0)
            dve.wait_ge(s_out2, 1)
            with dve.Fori(0, STEPS) as i:
                for a in range(2):
                    g = 2 * i + a + 1
                    dve.wait_ge(s_xn[a], 16 * i + 16)
                    dve.wait_ge(s_x[1 - a], 32 * (i + a) + 32)
                    for t in range(TILES):
                        for c in DVE_CHUNKS:
                            r = t * CHUNKS + c
                            for k in range(GROUPS):
                                if r == first_at(DVE_CHUNKS, SEL_AT[k]):
                                    product(g, 1 - a, k)
                            if r == first_at(DVE_CHUNKS, SUM_AT[-1] + 2):
                                low_x1(g, 1 - a)
                                sum_x1(g)
                            if (a, t, c) == (0, 1, 2):
                                save_out(i)
                            if (a, t, c) == (0, 1, 7):
                                save_out2(i)
                            weigh(i, a, t, c)
            dve.wait_ge(s_out0, MACROS + 2)
            dve.tensor_scalar(out0[:, 0:BATCH], out0[:, 0:BATCH], b0_16[:, 0:1], None, ALU.add).then_inc(s_last, 1)
            save_out(STEPS)
            save_out2(STEPS)

        @block.gpsimd
        def _(pool):
            def low_x(g, par):
                pool.wait_ge(s_xhi, g + 1)
                pool.tensor_tensor(xs_l[:, :], xs_f[par][:, :], xs_r[par][:, :].bitcast(F32),
                                   ALU.subtract).then_inc(s_xlo, 1)

            def add(out_, in0, in1, done):
                pool.wait_ge(s_chain, done)
                return pool.tensor_tensor(out_, in0, in1, ALU.add)

            pool.memset(x2[1][:, :], 0.0).then_inc(s_x2, 2)
            pool.memset(diag[1][:, :, :], 0.0).then_inc(s_diag, 1)
            pool.memset(acc_a[1][:, 0, 0:2], 0.0).then_inc(s_chain, CHAIN)
            pool.wait_ge(s_x[0], 32)
            low_x(0, 0)
            pool.wait_ge(s_consts, 7 * 16)
            with pool.Fori(0, STEPS) as i:
                for a in range(2):
                    g = 2 * i + a + 1
                    pool.wait_ge(s_x[1 - a], 32 * (i + a) + 32)
                    low_x(g, 1 - a)
                    pool.wait_ge(s_xn[a], 16 * i + 16)
                    for t in range(TILES):
                        tile = 2 * TILES * i + a * TILES + t
                        par = t % 2
                        pool.wait_ge(s_pair_sb, tile + 1)
                        pool.tensor_tensor(diag[par][:, :, :],
                                           xn[a][:, t, :].unsqueeze(2).to_broadcast([P, JX, TILE_B]),
                                           own_s[:, :].unsqueeze(1).to_broadcast([P, JX, TILE_B]),
                                           ALU.mult).then_inc(s_diag, 1)
                        whole = acc_a[par][:, :, :]
                        chained = CHAIN * (tile + 1)
                        for k in range(NA - 1):
                            pool.wait_ge(s_act, act_through(tile, ACT_CHUNKS[k + 1]))
                            add(whole, whole, prod[k][:, :, :], chained + k).then_inc(s_chain, 1)
                        pool.wait_ge(s_dve, dve_through(tile, DVE_CHUNKS[-1]))
                        add(whole, whole, acc_d[par][:, :, :], chained + NA - 1).then_inc(s_chain, 1)
                        add(acc_a[par][:, 0:2, :], acc_a[par][:, 0:2, :], acc_a[par][:, 2:4, :],
                            chained + NA).then_inc(s_chain, 1)
                        add(x2[par][:, :], acc_a[par][:, 0, :], acc_a[par][:, 1, :],
                            chained + CHAIN).then_inc(s_x2, 1)


def kernel(r_embedded_features, L0_rec_W0, L0_rec_b0, L0_rec_W1, L0_rec_b1, L0_rec_W2, L0_rec_b2):
    import concourse.bacc as bacc
    from concourse.bass_utils import run_bass_kernel_spmd

    x = np.asarray(r_embedded_features)
    f32 = x.dtype
    columns = x.transpose(1, 0, 2).reshape(FIELDS, COLS)
    pad = MACRO
    x_sel = np.zeros((P, COLS + pad), f32)
    x_sel[:FIELDS, :COLS] = columns
    x_sel[LOW:LOW + FIELDS, :COLS] = columns
    x_rep = np.zeros((P, COLS + pad), f32)
    x_rep[:COPIES * FIELDS, :COLS] = np.tile(columns, (COPIES, 1))
    x_row = np.zeros((MACROS + 1, P, TILES, JX), f32)
    x_row[:MACROS, :, :, :FIELDS] = x.transpose(0, 2, 1).reshape(MACROS, TILES, P, FIELDS).transpose(0, 2, 1, 3)
    x_row[:, :, :, FIELDS] = 1.0

    w0 = np.asarray(L0_rec_W0).reshape(HID, FIELDS, FIELDS)
    spread = np.zeros((P, GROUPS, P), f32)
    w0a = np.zeros((P, GROUPS, HID), f32)
    w0b = np.zeros((P, GROUPS, HID), f32)
    for t in range(GROUPS):
        for c in range(COPIES):
            shift = COPIES * t + c
            if shift >= SHIFTS:
                continue
            for k in range(FIELDS):
                row, other = c * FIELDS + k, (k + shift) % FIELDS
                spread[other, t, row] = spread[LOW + other, t, row] = 1.0
                w0a[row, t] = w0[:, k, other]
                if shift:
                    w0b[row, t] = w0[:, other, k]
    own = np.repeat(np.eye(TILE_B, dtype=f32), EMB, axis=0)

    def by_k(w):
        return w.reshape(HID, FIELDS, HID).transpose(2, 1, 0).reshape(HID, FIELDS * HID)

    given = {
        "x_sel": x_sel, "x_rep": x_rep, "x_row": x_row.reshape((MACROS + 1) * P, TILES * JX),
        "spread": spread.reshape(P, -1), "own": own, "w0a": w0a.reshape(P, -1), "w0b": w0b.reshape(P, -1),
        "w1": by_k(np.asarray(L0_rec_W1)), "w2": by_k(np.asarray(L0_rec_W2)),
        "b0": np.asarray(L0_rec_b0), "b1": np.asarray(L0_rec_b1), "b2": np.asarray(L0_rec_b2),
    }
    given = {name: np.ascontiguousarray(a) for name, a in given.items()}
    nc = bacc.Bacc("TRN2", target_bir_lowering=False, num_devices=1)
    aps = [nc.dram_tensor(name, a.shape, mybir.dt.from_np(a.dtype), kind="ExternalInput").ap()
           for name, a in given.items()]
    out = nc.dram_tensor("out", (3, HID, BATCH), F32, kind="ExternalOutput").ap()
    cin_kernel(nc, *aps, out)
    got = run_bass_kernel_spmd(nc, [given], core_ids=[0]).results[0]["out"]
    return got.transpose(2, 0, 1).reshape(BATCH, 3 * HID)
```

```python
from contextlib import ExitStack

import concourse.bass as bass
import numpy as np
from concourse import mybir

P = 128
BATCH, FIELDS, EMB = 1024, 39, 16
HID = 128
COLS = BATCH * EMB
TILE_B = P // EMB
STEP = 512
TILES = STEP // P
NSTEPS = COLS // STEP
PER_TRIP = 4
TRIPS = NSTEPS // PER_TRIP
TRIP_TILES = PER_TRIP * TILES
TRIP_B = TRIP_TILES * TILE_B
COPIES = P // FIELDS
ROWS = COPIES * FIELDS
SHIFTS = (FIELDS + 1) // 2
GROUPS = -(-SHIFTS // COPIES)
CJ = 4
CHUNKS = -(-FIELDS // CJ)
JX = FIELDS + 1
ACT_CHUNKS = tuple(range(0, CHUNKS, 2))
DVE_CHUNKS = tuple(range(1, CHUNKS, 2))
NA = len(ACT_CHUNKS)
ND = sum(min(CJ, FIELDS - CJ * c) for c in DVE_CHUNKS)
BANKS = 4
FORM_AT = [4 * g for g in range(GROUPS)]
ROUND_AT = [r + 1 for r in FORM_AT]
LOW_AT = [r + 2 for r in FORM_AT]
SUM_AT = [r + 6 for r in FORM_AT]
X1_AT = SUM_AT[-1] + 2
PAIR_AT, SAVE_AT = 6, 8
R_FROM, R_CHUNKS = CHUNKS - 1, 7

F32 = mybir.dt.float32
F32R = mybir.dt.float32r
ALU = mybir.AluOpType
ACT = mybir.ActivationFunctionType
AX_X = mybir.AxisListType.X


def fields_of(c):
    return slice(CJ * c, min(CJ * c + CJ, FIELDS))


def own_chunk(chunks, at):
    return min(t * CHUNKS + c for t in range(TILES) for c in chunks if t * CHUNKS + c >= at)


def act_through(tile, c):
    return NA * (tile + 1) + ACT_CHUNKS.index(c) + 1


def dve_through(tile, c):
    return ND * (tile + 1) + sum(fields_of(k).stop - fields_of(k).start for k in DVE_CHUNKS if k <= c)


def cin_kernel(nc, x_twice, x_rep, x_row, w0a, w0b, w1, w2, b0, b1, b2, out):
    with ExitStack() as ctx:
        def sb(name, shape, dt=F32):
            return ctx.enter_context(nc.sbuf_tensor(name, shape, dt))

        def psum(name, shape):
            return ctx.enter_context(nc.psum_tensor(name, shape, F32))

        def sem(name):
            return ctx.enter_context(nc.semaphore(name))

        y = [psum(f"y{b}", [P, CJ, HID]) for b in range(BANKS)]
        z = psum("z", [ROWS, STEP])
        x1_ps = psum("x1_ps", [P, STEP])
        pair_ps = psum("pair_ps", [P, TILE_B, JX])
        r_ps = psum("r_ps", [P, TRIP_B])

        w0_a = sb("w0_a", [ROWS, GROUPS, HID])
        w0_b = sb("w0_b", [ROWS, GROUPS, HID])
        w0_h = sb("w0_h", [ROWS, GROUPS, HID], F32R)
        w0_l = sb("w0_l", [ROWS, GROUPS, HID], F32R)
        w1_f = sb("w1_f", [P, FIELDS, HID])
        w1_h = sb("w1_h", [P, FIELDS, HID], F32R)
        w1_l = sb("w1_l", [P, FIELDS, HID], F32R)
        w2_s = sb("w2_s", [P, FIELDS, HID])
        b0_s = sb("b0_s", [P, 1])
        b0_16 = sb("b0_16", [P, 1])
        b1_row = sb("b1_row", [P, HID])
        b2_s = sb("b2_s", [P, 1])
        b2_16 = sb("b2_16", [P, 1])

        xs = [sb(f"xs{p}", [ROWS, GROUPS, STEP]) for p in range(2)]
        xr = [sb(f"xr{p}", [ROWS, STEP]) for p in range(2)]
        xn = [sb(f"xn{p}", [P, TILES, JX]) for p in range(2)]
        diag = [sb(f"diag{p}", [P, TILES, TILE_B, JX]) for p in range(2)]
        x1_h = [sb(f"x1_h{p}", [P, STEP], F32R) for p in range(2)]
        x1_l = [sb(f"x1_l{p}", [P, STEP], F32R) for p in range(2)]
        z_h = [sb(f"z_h{p}", [ROWS, STEP], F32R) for p in range(2)]
        z_l = [sb(f"z_l{p}", [ROWS, STEP], F32R) for p in range(2)]

        acc_d = [sb(f"acc_d{p}", [P, 2, HID]) for p in range(2)]
        acc_a = [sb(f"acc_a{p}", [P, CJ, HID]) for p in range(2)]
        prod = [sb(f"prod{p}", [P, CJ, HID]) for p in range(NA - 1)]
        x2 = [sb(f"x2_{p}", [P, HID]) for p in range(2)]
        pair = sb("pair", [P, JX, TRIP_B])
        out0 = sb("out0", [P, BATCH + STEP // EMB])
        out1 = sb("out1", [P, TRIP_B + BATCH])
        out2 = sb("out2", [P, TRIP_B + BATCH])

        s_consts = sem("s_consts")
        s_w1 = [sem(f"s_w1_{q}") for q in range(CHUNKS)]
        s_w2 = sem("s_w2")
        s_x = [sem(f"s_x{p}") for p in range(2)]
        s_xn = [sem(f"s_xn{p}") for p in range(2)]
        s_diag = [sem(f"s_diag{p}") for p in range(2)]
        s_clear = [sem(f"s_clear{p}") for p in range(2)]
        s_w0 = sem("s_w0")
        s_w0h = sem("s_w0h")
        s_w0l = sem("s_w0l")
        s_w1h = sem("s_w1h")
        s_w1l = sem("s_w1l")
        s_zero = sem("s_zero")
        s_z = sem("s_z")
        s_zh = sem("s_zh")
        s_zl = sem("s_zl")
        s_sum0 = sem("s_sum0")
        s_x1h = sem("s_x1h")
        s_x1l = sem("s_x1l")
        s_out0 = sem("s_out0")
        s_y = [sem(f"s_y{b}") for b in range(BANKS)]
        s_dve = sem("s_dve")
        s_act = sem("s_act")
        s_chain = sem("s_chain")
        s_x2 = sem("s_x2")
        s_pair = sem("s_pair")
        s_pair_sb = sem("s_pair_sb")
        s_r = sem("s_r")
        s_out1 = sem("s_out1")
        s_out2 = sem("s_out2")
        s_last = sem("s_last")
        s_store = sem("s_store")

        block = ctx.enter_context(nc.Block())
        CHAIN = NA + 1
        XCOLS = x_twice.shape[1]
        X_LOADS, DIAG_LOADS = 16 * (COPIES + 1), 16 * TILE_B

        def filled(i, q):
            return PER_TRIP * TILES * CHUNKS // BANKS * i + q // BANKS + 1

        @block.sync
        def _(sp):
            def load_x(g, par):
                cols = bass.ds(g * STEP, STEP)
                for c in range(COPIES):
                    rows = x_twice[c:c + FIELDS, cols]
                    src = bass.AP(tensor=rows.tensor, offset=rows.offset,
                                  ap=[[XCOLS, FIELDS], [COPIES * XCOLS, GROUPS], [1, STEP]])
                    sp.dma_start(xs[par][c * FIELDS:(c + 1) * FIELDS, :, :], src).then_inc(s_x[par], 16)
                sp.dma_start(xr[par][:, :], x_rep[:, cols]).then_inc(s_x[par], 16)

            def load_xn(g, par):
                sp.dma_start(xn[par][:, :, :], x_row[bass.ds(g * P, P), :, :]).then_inc(s_xn[par], 16)

            def load_diag(g, par):
                for b in range(TILE_B):
                    sp.dma_start(diag[par][b * EMB:(b + 1) * EMB, :, b, :],
                                 x_row[bass.ds(g * P + b * EMB, EMB), :, :]).then_inc(s_diag[par], 16)

            load_x(0, 0)
            for dst, src in ((w0_a, w0a), (w0_b, w0b)):
                sp.dma_start(dst[:, :, :].rearrange("p g m -> p (g m)"), src).then_inc(s_consts, 16)
            sp.dma_start(b0_s[:, :], b0.rearrange("(h o) -> h o", o=1)).then_inc(s_consts, 16)
            sp.dma_start(b2_s[:, :], b2.rearrange("(h o) -> h o", o=1)).then_inc(s_consts, 16)
            sp.dma_start(b1_row[:, :], b1.rearrange("(o h) -> o h", o=1).to_broadcast([P, HID])).then_inc(s_consts, 16)
            w1_v = w1.rearrange("k (j h) -> k j h", h=HID)
            for q in range(CHUNKS):
                sp.dma_start(w1_f[:, fields_of(q), :], w1_v[:, fields_of(q), :]).then_inc(s_w1[q], 16)
            load_xn(0, 0)
            sp.wait_ge(s_clear[0], 1)
            load_diag(0, 0)
            sp.dma_start(w2_s[:, :, :].rearrange("p j h -> p (j h)"), w2).then_inc(s_w2, 16)
            with sp.Fori(0, TRIPS) as i:
                for a in range(PER_TRIP):
                    g, par = PER_TRIP * i + a + 1, (a + 1) % 2
                    sp.wait_ge(s_out0, g)
                    load_x(g, par)
                    sp.wait_ge(s_dve, TILES * ND * (g - 1) + ND)
                    sp.wait_ge(s_act, TILES * NA * (g - 1) + NA)
                    load_xn(g, par)
                    sp.wait_ge(s_pair, TILES * (g - 1) + 1)
                    load_diag(g, par)
            sp.wait_ge(s_last, 1)
            sp.dma_start(out[0], out0[:, 0:BATCH]).then_inc(s_store, 16)
            sp.wait_ge(s_out1, TRIPS + 1)
            sp.dma_start(out[1], out1[:, TRIP_B:]).then_inc(s_store, 16)
            sp.wait_ge(s_out2, TRIPS + 2)
            sp.dma_start(out[2], out2[:, TRIP_B:]).then_inc(s_store, 16)
            sp.wait_ge(s_store, 48)

        @block.tensor
        def _(pe):
            def split_matmul(out_, w_h, w_l, m_h, m_l, start, stop):
                pe.matmul(out_, w_h, m_h, start=start, stop=False)
                pe.matmul(out_, w_h, m_l, start=False, stop=False)
                return pe.matmul(out_, w_l, m_h, start=False, stop=stop)

            def sum_products(g, odd, t):
                par = (odd + t) % 2
                pe.wait_ge(s_zl, GROUPS * g + t + 1)
                if t == 0:
                    pe.wait_ge(s_out0, g + 1)
                split_matmul(x1_ps[:, :], w0_h[:, t, :], w0_l[:, t, :], z_h[par][:, :], z_l[par][:, :],
                             t == 0, t == GROUPS - 1).then_inc(s_sum0, 1)

            def layer1(i, a, t, c):
                q = (a * TILES + t) * CHUNKS + c
                bank = q % BANKS
                tile, before = TRIP_TILES * i + (q - BANKS) // CHUNKS, (q - BANKS) % CHUNKS
                if before in ACT_CHUNKS:
                    pe.wait_ge(s_act, act_through(tile, before))
                else:
                    pe.wait_ge(s_dve, dve_through(tile, before))
                js, cols = fields_of(c), slice(t * P, t * P + P)
                split_matmul(y[bank][:, 0:js.stop - js.start, :], x1_h[a % 2][:, cols], x1_l[a % 2][:, cols],
                             w1_h[:, js, :], w1_l[:, js, :], True, True).then_inc(s_y[bank], 1)

            def pair_sums(tile, u):
                pe.wait_ge(s_x2, tile + 3)
                pe.wait_ge(s_pair_sb, tile + 2)
                pe.matmul(pair_ps[:, :, :], x2[u % 2][:, :], diag[u // TILES % 2][:, u % TILES, :, :],
                          start=True, stop=True).then_inc(s_pair, 1)

            def layer2(i, js):
                if js.start == 0:
                    pe.wait_ge(s_pair_sb, TRIP_TILES * i + 2)
                    pe.wait_ge(s_out2, i + 1)
                for j in range(js.start, js.stop):
                    last = pe.matmul(r_ps[:, :], w2_s[:, j, :], pair[:, j, :],
                                     start=(j == 0), stop=(j == FIELDS - 1))
                if js.stop == FIELDS:
                    last.then_inc(s_r, 1)

            pe.wait_ge(s_w0h, 1)
            pe.wait_ge(s_w0l, 1)
            for t in range(GROUPS):
                sum_products(0, 0, t)
            pe.wait_ge(s_zero, 1)
            pe.wait_ge(s_clear[1], 1)
            pe.wait_ge(s_w1h, CHUNKS)
            pe.wait_ge(s_w1l, CHUNKS)
            pe.wait_ge(s_w2, 16)
            with pe.Fori(0, TRIPS) as i:
                for a in range(PER_TRIP):
                    g = PER_TRIP * i + a + 1
                    pe.wait_ge(s_x1l, g)
                    for t in range(TILES):
                        u = a * TILES + t
                        for c in range(CHUNKS):
                            r = t * CHUNKS + c
                            if r in SUM_AT:
                                sum_products(g, a + 1, SUM_AT.index(r))
                            if c == PAIR_AT:
                                if t == 1:
                                    pe.wait_ge(s_diag[a % 2], DIAG_LOADS * (PER_TRIP // 2 * i + a // 2 + 1))
                                pair_sums(TRIP_TILES * i + u - 1, (u - 1) % TRIP_TILES)
                            n = u * CHUNKS + c - R_FROM
                            if 0 <= n < R_CHUNKS:
                                layer2(i, slice(n * FIELDS // R_CHUNKS, (n + 1) * FIELDS // R_CHUNKS))
                            layer1(i, a, t, c)
            pair_sums(TRIPS * TRIP_TILES - 1, TRIP_TILES - 1)
            layer2(TRIPS, slice(0, FIELDS))

        @block.scalar
        def _(act):
            def round_z(g, odd, t):
                par = (odd + t) % 2
                act.wait_ge(s_z, GROUPS * g + t + 1)
                if not isinstance(g, int) or t > 1:
                    act.wait_ge(s_sum0, GROUPS * g + t - 1)
                act.activation(z_h[par][:, :], z[:, :], ACT.Copy).then_inc(s_zh, 1)

            def round_x1(g, par):
                act.wait_ge(s_sum0, GROUPS * g + GROUPS)
                act.activation(x1_h[par][:, :], x1_ps[:, :], ACT.Identity, bias=b0_s[:, 0:1]).then_inc(s_x1h, 1)

            def weigh(i, a, t, c):
                q = (a * TILES + t) * CHUNKS + c
                bank = q % BANKS
                tile = TRIP_TILES * i + a * TILES + t
                k = ACT_CHUNKS.index(c)
                if k == 0:
                    act.wait_ge(s_x2, tile + 1)
                    dst = acc_a[t % 2]
                else:
                    act.wait_ge(s_chain, CHAIN * tile + k)
                    dst = prod[k - 1]
                act.wait_ge(s_y[bank], filled(i, q))
                for s in range(CJ):
                    last = act.activation(dst[:, s, :], y[bank][:, s, :], ACT.Copy,
                                          scale=xn[a % 2][:, t, CJ * c + s:CJ * c + s + 1])
                last.then_inc(s_act, 1)

            def save_pair(tile, u):
                act.wait_ge(s_pair, tile + 2)
                act.activation(pair[:, :, TILE_B * u:TILE_B * u + TILE_B],
                               pair_ps[:, :, :].rearrange("k b j -> k j b"), ACT.Copy).then_inc(s_pair_sb, 1)

            act.wait_ge(s_w0, 1)
            act.activation(w0_h[:, :, :], w0_a[:, :, :], ACT.Copy).then_inc(s_w0h, 1)
            act.activation(prod[-1][0:ROWS, 0, 0:2], w0_a[:, 0, 0:2], ACT.Copy).then_inc(s_act, NA)
            act.activation(prod[-1][0:ROWS, 1, 0:2], w0_a[:, 0, 0:2], ACT.Copy).then_inc(s_pair_sb, 1)
            act.wait_ge(s_consts, 5 * 16)
            for t in range(GROUPS):
                round_z(0, 0, t)
            for q in range(CHUNKS):
                act.wait_ge(s_w1[q], 16)
                act.activation(w1_h[:, fields_of(q), :], w1_f[:, fields_of(q), :], ACT.Copy).then_inc(s_w1h, 1)
                if q == 1:
                    round_x1(0, 0)
            act.wait_ge(s_zero, 1)
            with act.Fori(0, TRIPS) as i:
                for a in range(PER_TRIP):
                    g = PER_TRIP * i + a + 1
                    act.wait_ge(s_xn[a % 2], 16 * (PER_TRIP // 2 * i + a // 2) + 16)
                    for t in range(TILES):
                        u = a * TILES + t
                        for c in ACT_CHUNKS:
                            r = t * CHUNKS + c
                            for k in range(GROUPS):
                                if r == own_chunk(ACT_CHUNKS, ROUND_AT[k]):
                                    round_z(g, a + 1, k)
                            if r == own_chunk(ACT_CHUNKS, X1_AT):
                                round_x1(g, (a + 1) % 2)
                            if c == SAVE_AT:
                                if u == 1:
                                    act.wait_ge(s_out1, i + 1)
                                save_pair(TRIP_TILES * i + u - 1, (u - 1) % TRIP_TILES)
                            weigh(i, a, t, c)
            save_pair(TRIPS * TRIP_TILES - 1, TRIP_TILES - 1)

        @block.vector
        def _(dve):
            def form_z(g, par, t):
                if not isinstance(g, int) or t > 0:
                    dve.wait_ge(s_zl, GROUPS * g + t)
                dve.tensor_tensor(z[:, :], xs[par][:, t, :], xr[par][:, :], ALU.mult).then_inc(s_z, 1)

            def low_z(g, odd, t):
                par = (odd + t) % 2
                dve.wait_ge(s_zh, GROUPS * g + t + 1)
                dve.tensor_tensor(z_l[par][:, :], z[:, :], z_h[par][:, :].bitcast(F32),
                                  ALU.subtract).then_inc(s_zl, 1)

            def low_x1(g, par):
                dve.wait_ge(s_x1h, g + 1)
                dve.scalar_tensor_tensor(out=x1_l[par][:, :], in0=x1_ps[:, :], scalar=b0_s[:, 0:1],
                                         in1=x1_h[par][:, :].bitcast(F32), op0=ALU.add,
                                         op1=ALU.subtract).then_inc(s_x1l, 1)
                dve.tensor_reduce(out0[:, bass.ds(g * (STEP // EMB), STEP // EMB)],
                                  x1_ps[:, :].rearrange("h (b d) -> h b d", d=EMB), AX_X,
                                  ALU.add).then_inc(s_out0, 1)

            def weigh(i, a, t, c):
                q = (a * TILES + t) * CHUNKS + c
                bank = q % BANKS
                tile = TRIP_TILES * i + a * TILES + t
                done = dve_through(tile - 1, DVE_CHUNKS[-1])
                for s in range(fields_of(c).stop - fields_of(c).start):
                    x = xn[a % 2][:, t, CJ * c + s:CJ * c + s + 1]
                    f = CJ * DVE_CHUNKS.index(c) + s
                    acc = acc_d[t % 2][:, f % 2, :]
                    if f == 0:
                        dve.wait_ge(s_x2, tile + 1)
                    if s == 0:
                        dve.wait_ge(s_y[bank], filled(i, q))
                    if f > 1:
                        dve.wait_ge(s_dve, done + f - 1)
                    if f == 1:
                        step = dve.tensor_scalar(acc, y[bank][:, s, :], x, None, ALU.mult)
                    else:
                        step = dve.scalar_tensor_tensor(out=acc, in0=y[bank][:, s, :], scalar=x,
                                                        in1=acc if f else b1_row[:, :],
                                                        op0=ALU.mult, op1=ALU.add)
                    step.then_inc(s_dve, 1)

            def save_out1(i):
                dve.wait_ge(s_pair_sb, TRIP_TILES * i + 2)
                dve.tensor_scalar(out1[:, bass.ds(i * TRIP_B, TRIP_B)], pair[:, FIELDS, :], 1.0, None,
                                  ALU.mult).then_inc(s_out1, 1)

            def save_out2(i):
                dve.wait_ge(s_r, i + 1)
                dve.tensor_scalar(out2[:, bass.ds(i * TRIP_B, TRIP_B)], r_ps[:, :], b2_16[:, 0:1], None,
                                  ALU.add).then_inc(s_out2, 1)

            dve.wait_ge(s_consts, 5 * 16)
            dve.tensor_tensor(w0_a[:, :, :], w0_a[:, :, :], w0_b[:, :, :], ALU.add).then_inc(s_w0, 1)
            dve.wait_ge(s_w0h, 1)
            dve.tensor_tensor(w0_l[:, :, :], w0_a[:, :, :], w0_h[:, :, :].bitcast(F32),
                              ALU.subtract).then_inc(s_w0l, 1)
            dve.tensor_scalar(b0_16[:, :], b0_s[:, :], float(EMB), None, ALU.mult).then_inc(s_out0, 1)
            dve.tensor_scalar(b2_16[:, :], b2_s[:, :], float(EMB), None, ALU.mult).then_inc(s_out2, 1)
            dve.wait_ge(s_x[0], X_LOADS)
            for t in range(GROUPS):
                form_z(0, 0, t)
                if t > 1:
                    dve.wait_ge(s_sum0, t - 1)
                low_z(0, 0, t)
            for q in range(CHUNKS):
                dve.wait_ge(s_w1h, q + 1)
                dve.tensor_tensor(w1_l[:, fields_of(q), :], w1_f[:, fields_of(q), :],
                                  w1_h[:, fields_of(q), :].bitcast(F32), ALU.subtract).then_inc(s_w1l, 1)
                if q == 1:
                    low_x1(0, 0)
            dve.memset(acc_d[1][:, 0, 0:2], 0.0).then_inc(s_dve, ND)
            dve.wait_ge(s_out2, 1)
            with dve.Fori(0, TRIPS) as i:
                for a in range(PER_TRIP):
                    g, par = PER_TRIP * i + a + 1, (a + 1) % 2
                    dve.wait_ge(s_xn[a % 2], 16 * (PER_TRIP // 2 * i + a // 2) + 16)
                    for t in range(TILES):
                        u = a * TILES + t
                        for c in DVE_CHUNKS:
                            r = t * CHUNKS + c
                            for k in range(GROUPS):
                                if r == own_chunk(DVE_CHUNKS, LOW_AT[k]):
                                    low_z(g, a + 1, k)
                            for k in range(GROUPS):
                                if r == own_chunk(DVE_CHUNKS, FORM_AT[k]):
                                    if k == 0:
                                        dve.wait_ge(s_x[par], X_LOADS * (PER_TRIP // 2 * i + (a + 1) // 2 + 1))
                                    form_z(g, par, k)
                            if r == own_chunk(DVE_CHUNKS, X1_AT + 1):
                                low_x1(g, par)
                            if (u, c) == (0, 9):
                                save_out1(i)
                            if (u, c) == (1, 9):
                                save_out2(i)
                            weigh(i, a, t, c)
            dve.wait_ge(s_out0, NSTEPS + 2)
            dve.tensor_scalar(out0[:, 0:BATCH], out0[:, 0:BATCH], b0_16[:, 0:1], None, ALU.add).then_inc(s_last, 1)
            save_out1(TRIPS)
            save_out2(TRIPS)

        @block.gpsimd
        def _(pool):
            def add(out_, in0, in1, done):
                pool.wait_ge(s_chain, done)
                return pool.tensor_tensor(out_, in0, in1, ALU.add)

            pool.memset(diag[0][:, :, :, :], 0.0).then_inc(s_clear[0], 1)
            pool.memset(x2[1][:, :], 0.0).then_inc(s_x2, 2)
            pool.memset(diag[1][:, :, :, :], 0.0).then_inc(s_clear[1], 1)
            pool.memset(pair[:, :, :], 0.0).then_inc(s_zero, 1)
            pool.memset(acc_a[1][:, 0, 0:2], 0.0).then_inc(s_chain, CHAIN)
            with pool.Fori(0, TRIPS) as i:
                for u in range(TRIP_TILES):
                    tile, par = TRIP_TILES * i + u, u % 2
                    whole, half = acc_a[par][:, :, :], acc_a[par][:, 0:2, :]
                    chained = CHAIN * (tile + 1)
                    for k in range(NA - 1):
                        pool.wait_ge(s_act, act_through(tile, ACT_CHUNKS[k + 1]))
                        add(whole, whole, prod[k][:, :, :], chained + k).then_inc(s_chain, 1)
                    add(half, half, acc_a[par][:, 2:4, :], chained + NA - 1).then_inc(s_chain, 1)
                    pool.wait_ge(s_dve, dve_through(tile, DVE_CHUNKS[-1]))
                    add(half, half, acc_d[par][:, :, :], chained + NA).then_inc(s_chain, 1)
                    pool.wait_ge(s_pair_sb, tile + 1)
                    add(x2[par][:, :], acc_a[par][:, 0, :], acc_a[par][:, 1, :],
                        chained + CHAIN).then_inc(s_x2, 1)


def kernel(r_embedded_features, L0_rec_W0, L0_rec_b0, L0_rec_W1, L0_rec_b1, L0_rec_W2, L0_rec_b2):
    import concourse.bacc as bacc
    from concourse.bass_utils import run_bass_kernel_spmd

    x = np.asarray(r_embedded_features)
    f32 = x.dtype
    padded = COLS + STEP
    columns = np.zeros((FIELDS, padded), f32)
    columns[:, :COLS] = x.transpose(1, 0, 2).reshape(FIELDS, COLS)
    x_twice = np.concatenate([columns, columns])
    x_rep = np.tile(columns, (COPIES, 1))
    x_row = np.zeros((NSTEPS + 1, P, TILES, JX), f32)
    x_row[:NSTEPS, :, :, :FIELDS] = x.transpose(0, 2, 1).reshape(NSTEPS, TILES, P, FIELDS).transpose(0, 2, 1, 3)
    x_row[:, :, :, FIELDS] = 1.0

    w0 = np.asarray(L0_rec_W0).reshape(HID, FIELDS, FIELDS)
    w0a = np.zeros((ROWS, GROUPS, HID), f32)
    w0b = np.zeros((ROWS, GROUPS, HID), f32)
    for shift in range(SHIFTS):
        t, c = divmod(shift, COPIES)
        for k in range(FIELDS):
            row, other = c * FIELDS + k, (k + shift) % FIELDS
            w0a[row, t] = w0[:, k, other]
            if shift:
                w0b[row, t] = w0[:, other, k]

    def by_k(w):
        return w.reshape(HID, FIELDS, HID).transpose(2, 1, 0).reshape(HID, FIELDS * HID)

    given = {
        "x_twice": x_twice, "x_rep": x_rep, "x_row": x_row.reshape((NSTEPS + 1) * P, TILES, JX),
        "w0a": w0a.reshape(ROWS, -1), "w0b": w0b.reshape(ROWS, -1),
        "w1": by_k(np.asarray(L0_rec_W1)), "w2": by_k(np.asarray(L0_rec_W2)),
        "b0": np.asarray(L0_rec_b0), "b1": np.asarray(L0_rec_b1), "b2": np.asarray(L0_rec_b2),
    }
    given = {name: np.ascontiguousarray(a) for name, a in given.items()}
    nc = bacc.Bacc("TRN2", target_bir_lowering=False, num_devices=1)
    aps = [nc.dram_tensor(name, a.shape, mybir.dt.from_np(a.dtype), kind="ExternalInput").ap()
           for name, a in given.items()]
    out = nc.dram_tensor("out", (3, HID, BATCH), F32, kind="ExternalOutput").ap()
    cin_kernel(nc, *aps, out)
    got = run_bass_kernel_spmd(nc, [given], core_ids=[0]).results[0]["out"]
    return got.transpose(2, 0, 1).reshape(BATCH, 3 * HID)
```

```python
from contextlib import ExitStack

import concourse.bass as bass
import numpy as np
from concourse import mybir

P = 128
BATCH, FIELDS, EMB = 1024, 39, 16
HID = 128
COLS = BATCH * EMB
TILE_B = P // EMB
STEP = 512
TILES = STEP // P
NSTEPS = COLS // STEP
PER_TRIP = 4
TRIPS = NSTEPS // PER_TRIP
TRIP_TILES = PER_TRIP * TILES
TRIP_B = TRIP_TILES * TILE_B
COPIES = P // FIELDS
ROWS = COPIES * FIELDS
EXTRA = P - ROWS
FULL = (FIELDS + 1) // 2 // COPIES
GROUPS = FULL + 1
FIRST_EXTRA = FULL * COPIES


def product_pairs():
    seen, tiles = set(), []
    for t in range(FULL):
        rows = [(k, (k + COPIES * t + c) % FIELDS) for c in range(COPIES) for k in range(FIELDS)]
        extra = [(k, (k + FIRST_EXTRA + t) % FIELDS) for k in range(EXTRA)]
        if FIRST_EXTRA + t > FIELDS - FIRST_EXTRA:
            extra = [None] * EXTRA
        tiles.append(rows + extra)
        seen.update(frozenset(pair) for pair in tiles[-1] if pair)
    return tiles, [(k, j) for k in range(FIELDS) for j in range(k, FIELDS) if frozenset((k, j)) not in seen]


FULL_PAIRS, LEFT = product_pairs()
NL, LOW_ROW = len(LEFT), 64
LAST_ROWS = 3 * NL
LAST_PAIRS = LEFT + LEFT[:LOW_ROW - NL] + LEFT + LEFT[LOW_ROW - NL:]
CJ = 4
CHUNKS = -(-FIELDS // CJ)
JX = FIELDS + 1
ACT_CHUNKS = tuple(range(0, CHUNKS, 2))
DVE_CHUNKS = tuple(range(1, CHUNKS, 2))
NA = len(ACT_CHUNKS)
ND = sum(min(CJ, FIELDS - CJ * c) for c in DVE_CHUNKS)
BANKS = 4
FORM_AT = [4 * g for g in range(GROUPS)]
ROUND_AT = [r + 1 for r in FORM_AT]
LOW_AT = [r + 2 for r in FORM_AT]
SUM_AT = [r + 6 for r in FORM_AT]
X1_AT = SUM_AT[-1] + 2
OUT0_AT = X1_AT + 7
SPLIT_AT, PAIR_AT, SAVE_AT = 6, 4, 6
R_FROM, R_CHUNKS = CHUNKS + 8, 6

F32 = mybir.dt.float32
F32R = mybir.dt.float32r
ALU = mybir.AluOpType
ACT = mybir.ActivationFunctionType
AX_X = mybir.AxisListType.X


def fields_of(c):
    return slice(CJ * c, min(CJ * c + CJ, FIELDS))


def own_chunk(chunks, at):
    return min(t * CHUNKS + c for t in range(TILES) for c in chunks if t * CHUNKS + c >= at)


def act_through(tile, c):
    return NA * (tile + 1) + ACT_CHUNKS.index(c) + 1


def dve_through(tile, c):
    return ND * (tile + 1) + sum(fields_of(k).stop - fields_of(k).start for k in DVE_CHUNKS if k <= c)


def cin_kernel(nc, x_twice, x_rep, x_last, x_row, w0a, w0b, w1, w2, b0, b1, b2, out):
    with ExitStack() as ctx:
        def sb(name, shape, dt=F32):
            return ctx.enter_context(nc.sbuf_tensor(name, shape, dt))

        def psum(name, shape):
            return ctx.enter_context(nc.psum_tensor(name, shape, F32))

        def sem(name):
            return ctx.enter_context(nc.semaphore(name))

        y = [psum(f"y{b}", [P, CJ, HID]) for b in range(BANKS)]
        z = psum("z", [P, STEP])
        x1_ps = psum("x1_ps", [P, STEP])
        pair_ps = psum("pair_ps", [P, TILE_B, JX])
        r_ps = psum("r_ps", [P, TRIP_B])

        w0_a = sb("w0_a", [P, GROUPS, HID])
        w0_b = sb("w0_b", [P, GROUPS, HID])
        w0_h = sb("w0_h", [P, GROUPS, HID], F32R)
        w0_l = sb("w0_l", [P, GROUPS, HID], F32R)
        w1_h = sb("w1_h", [P, FIELDS, HID], F32R)
        w1_l = sb("w1_l", [P, FIELDS, HID], F32R)
        w2_s = sb("w2_s", [P, FIELDS, HID])
        b0_s = sb("b0_s", [P, 1])
        b0_16 = sb("b0_16", [P, 1])
        b1_row = sb("b1_row", [P, HID])
        b2_s = sb("b2_s", [P, 1])
        b2_16 = sb("b2_16", [P, 1])

        xs = [sb(f"xs{p}", [P, FULL, STEP]) for p in range(2)]
        xr = [sb(f"xr{p}", [P, STEP]) for p in range(2)]
        xl = [sb(f"xl{p}", [LAST_ROWS, 2, STEP]) for p in range(2)]
        xn = [sb(f"xn{p}", [P, TILES, JX]) for p in range(2)]
        xn_h = [sb(f"xn_h{p}", [P, TILES, JX], F32R) for p in range(2)]
        xn_l = [sb(f"xn_l{p}", [P, TILES, JX], F32R) for p in range(2)]
        diag_h = [sb(f"diag_h{p}", [P, TILES, TILE_B, JX], F32R) for p in range(2)]
        diag_l = [sb(f"diag_l{p}", [P, TILES, TILE_B, JX], F32R) for p in range(2)]
        x1_h = [sb(f"x1_h{p}", [P, STEP], F32R) for p in range(2)]
        x1_l = [sb(f"x1_l{p}", [P, STEP], F32R) for p in range(2)]
        z_h = [sb(f"z_h{p}", [P, STEP], F32R) for p in range(2)]
        z_l = [sb(f"z_l{p}", [P, STEP], F32R) for p in range(2)]

        acc_d = [sb(f"acc_d{p}", [P, 2, HID]) for p in range(2)]
        acc_a = [sb(f"acc_a{p}", [P, CJ, HID]) for p in range(2)]
        prod = [sb(f"prod{p}", [P, CJ, HID]) for p in range(NA - 1)]
        x2 = [sb(f"x2_{p}", [P, HID]) for p in range(2)]
        x2_h = [sb(f"x2_h{p}", [P, HID], F32R) for p in range(2)]
        x2_l = [sb(f"x2_l{p}", [P, HID], F32R) for p in range(2)]
        pair = sb("pair", [P, JX, TRIP_B])
        w1_f = pair[:, 0:FIELDS, :]
        out0 = sb("out0", [P, BATCH + STEP // EMB])
        out1 = sb("out1", [P, TRIP_B + BATCH])
        out2 = sb("out2", [P, TRIP_B + BATCH])

        s_w0_in = sem("s_w0_in")
        s_consts = sem("s_consts")
        s_w1 = [sem(f"s_w1_{q}") for q in range(CHUNKS)]
        s_w2 = sem("s_w2")
        s_first = [sem(f"s_first{q}") for q in range(2)]
        s_x = [sem(f"s_x{p}") for p in range(2)]
        s_xn = [sem(f"s_xn{p}") for p in range(2)]
        s_diag = [sem(f"s_diag{p}") for p in range(2)]
        s_clear = sem("s_clear")
        s_w0 = sem("s_w0")
        s_w0h = sem("s_w0h")
        s_w0l = sem("s_w0l")
        s_w1h = sem("s_w1h")
        s_w1l = sem("s_w1l")
        s_ones = sem("s_ones")
        s_z = sem("s_z")
        s_zh = sem("s_zh")
        s_zl = sem("s_zl")
        s_sum0 = sem("s_sum0")
        s_x1h = sem("s_x1h")
        s_x1l = sem("s_x1l")
        s_out0 = sem("s_out0")
        s_y = [sem(f"s_y{b}") for b in range(BANKS)]
        s_dve = sem("s_dve")
        s_act = sem("s_act")
        s_chain = sem("s_chain")
        s_x2 = sem("s_x2")
        s_x2h = sem("s_x2h")
        s_x2l = sem("s_x2l")
        s_xnh = sem("s_xnh")
        s_xnl = sem("s_xnl")
        s_pair = sem("s_pair")
        s_pair_sb = sem("s_pair_sb")
        s_r = sem("s_r")
        s_out1 = sem("s_out1")
        s_out2 = sem("s_out2")
        s_last = sem("s_last")
        s_store = sem("s_store")

        block = ctx.enter_context(nc.Block())
        z_first = [z[:, :], y[0][:, :, :].rearrange("p j h -> p (j h)")]
        LOW_AFTER = 2
        CHAIN = NA + 1
        XCOLS = x_twice.shape[1]
        X_LOADS, DIAG_LOADS = 16 * (COPIES + 3), 16 * 2 * TILE_B
        FIRST_TILES = 2

        def filled(i, q):
            return PER_TRIP * TILES * CHUNKS // BANKS * i + q // BANKS + 1

        @block.sync
        def _(sp):
            def load_shifted(g, par, start, stop, done):
                cols = bass.ds(g * STEP, STEP)
                for c in range(COPIES + 1):
                    n, shift, each = ((FIELDS, COPIES * start + c, COPIES) if c < COPIES else
                                      (EXTRA, FIRST_EXTRA + start, 1))
                    rows = x_twice[shift:shift + n, cols]
                    src = bass.AP(tensor=rows.tensor, offset=rows.offset,
                                  ap=[[XCOLS, n], [each * XCOLS, stop - start], [1, STEP]])
                    sp.dma_start(xs[par][c * FIELDS:c * FIELDS + n, start:stop, :], src).then_inc(done, 16)

            def load_plain(g, par, done):
                sp.dma_start(xr[par][:, :], x_rep[:, bass.ds(g * STEP, STEP)]).then_inc(done, 16)

            def load_last(g, par, done):
                sp.dma_start(xl[par][:, :, :], x_last[:, :, bass.ds(g * STEP, STEP)]).then_inc(done, 16)

            def load_x(g, par):
                load_shifted(g, par, 0, FULL, s_x[par])
                load_plain(g, par, s_x[par])
                load_last(g, par, s_x[par])

            def load_xn(g, par):
                sp.dma_start(xn[par][:, :, :], x_row[bass.ds(g * P, P), :, :]).then_inc(s_xn[par], 16)

            def place_diag(g, par):
                sp.wait_ge(s_xnl, g + 1)
                for diag, parts in ((diag_h, xn_h), (diag_l, xn_l)):
                    for b in range(TILE_B):
                        rows = slice(b * EMB, (b + 1) * EMB)
                        sp.dma_start(diag[par][rows, :, b, :].bitcast(F32),
                                     parts[par][rows, :, :].bitcast(F32)).then_inc(s_diag[par], 16)

            for dst, src in ((w0_a, w0a), (w0_b, w0b)):
                sp.dma_start(dst[:, :, :].rearrange("p g m -> p (g m)"), src).then_inc(s_w0_in, 16)
            load_plain(0, 0, s_first[0])
            load_shifted(0, 0, 0, FIRST_TILES, s_first[0])
            load_shifted(0, 0, FIRST_TILES, FULL, s_first[1])
            load_last(0, 0, s_first[1])
            sp.dma_start(b0_s[:, :], b0.rearrange("(h o) -> h o", o=1)).then_inc(s_consts, 16)
            sp.dma_start(b2_s[:, :], b2.rearrange("(h o) -> h o", o=1)).then_inc(s_consts, 16)
            sp.dma_start(b1_row[:, :], b1.rearrange("(o h) -> o h", o=1).to_broadcast([P, HID])).then_inc(s_consts, 16)
            load_xn(0, 0)
            w1_v = w1.rearrange("k (j h) -> k j h", h=HID)
            for q in range(CHUNKS):
                sp.dma_start(w1_f[:, fields_of(q), :], w1_v[:, fields_of(q), :]).then_inc(s_w1[q], 16)
            load_x(1, 1)
            sp.dma_start(w2_s[:, :, :].rearrange("p j h -> p (j h)"), w2).then_inc(s_w2, 16)
            sp.wait_ge(s_clear, 4)
            place_diag(0, 0)
            with sp.Fori(0, TRIPS) as i:
                for a in range(PER_TRIP):
                    g, par = PER_TRIP * i + a + 1, (a + 1) % 2
                    sp.wait_ge(s_out0, g + 1)
                    load_x(g + 1, 1 - par)
                    sp.wait_ge(s_dve, TILES * ND * (g - 1) + ND)
                    sp.wait_ge(s_act, TILES * NA * (g - 1) + NA)
                    load_xn(g, par)
                    place_diag(g, par)
            sp.wait_ge(s_x[(NSTEPS + 1) % 2], X_LOADS * (NSTEPS // 2 + 1))
            sp.wait_ge(s_diag[NSTEPS % 2], DIAG_LOADS * (NSTEPS // 2 + 1))
            sp.wait_ge(s_last, 1)
            sp.dma_start(out[0], out0[:, 0:BATCH]).then_inc(s_store, 16)
            sp.wait_ge(s_out1, TRIPS + 1)
            sp.dma_start(out[1], out1[:, TRIP_B:]).then_inc(s_store, 16)
            sp.wait_ge(s_out2, TRIPS + 2)
            sp.dma_start(out[2], out2[:, TRIP_B:]).then_inc(s_store, 16)
            sp.wait_ge(s_store, 48)

        @block.tensor
        def _(pe):
            def split_matmul(out_, w_h, w_l, m_h, m_l, start, stop):
                pe.matmul(out_, w_h, m_h, start=start, stop=False)
                pe.matmul(out_, w_h, m_l, start=False, stop=False)
                return pe.matmul(out_, w_l, m_h, start=False, stop=stop)

            def sum_products(g, odd, t):
                par = (odd + t) % 2
                pe.wait_ge(s_zl, GROUPS * g + t + 1)
                if t == 0 and not isinstance(g, int):
                    pe.wait_ge(s_out0, g + 1)
                if t < FULL:
                    split_matmul(x1_ps[:, :], w0_h[:, t, :], w0_l[:, t, :], z_h[par][:, :], z_l[par][:, :],
                                 t == 0, False).then_inc(s_sum0, 1)
                else:
                    pe.matmul(x1_ps[:, :], w0_l[0:LAST_ROWS, t, :], z_h[par][0:LAST_ROWS, :],
                              start=False, stop=True).then_inc(s_sum0, 1)

            def layer1(i, a, t, c):
                q = (a * TILES + t) * CHUNKS + c
                bank = q % BANKS
                tile, before = TRIP_TILES * i + (q - BANKS) // CHUNKS, (q - BANKS) % CHUNKS
                if before in ACT_CHUNKS:
                    pe.wait_ge(s_act, act_through(tile, before))
                else:
                    pe.wait_ge(s_dve, dve_through(tile, before))
                js, cols = fields_of(c), slice(t * P, t * P + P)
                split_matmul(y[bank][:, 0:js.stop - js.start, :], x1_h[a % 2][:, cols], x1_l[a % 2][:, cols],
                             w1_h[:, js, :], w1_l[:, js, :], True, True).then_inc(s_y[bank], 1)

            def pair_sums(tile, u):
                pe.wait_ge(s_x2l, tile + 3)
                pe.wait_ge(s_pair_sb, tile + 3)
                par, t = u // TILES % 2, u % TILES
                split_matmul(pair_ps[:, :, :], x2_h[u % 2][:, :], x2_l[u % 2][:, :],
                             diag_h[par][:, t, :, :], diag_l[par][:, t, :, :], True, True).then_inc(s_pair, 1)

            def layer2(i, js):
                if js.start == 0:
                    pe.wait_ge(s_pair_sb, TRIP_TILES * i + 3)
                    pe.wait_ge(s_out2, i + 1)
                    pe.wait_ge(s_w2, 16)
                for j in range(js.start, js.stop):
                    last = pe.matmul(r_ps[:, :], w2_s[:, j, :], pair[:, j, :],
                                     start=(j == 0), stop=(j == FIELDS - 1))
                if js.stop == FIELDS:
                    last.then_inc(s_r, 1)

            pe.wait_ge(s_w0h, 1)
            pe.wait_ge(s_w0l, 1)
            for t in range(GROUPS):
                if t == FULL:
                    pe.wait_ge(s_w0h, 3)
                sum_products(0, 0, t)
            pe.wait_ge(s_clear, 5)
            with pe.Fori(0, TRIPS) as i:
                for a in range(PER_TRIP):
                    g = PER_TRIP * i + a + 1
                    pe.wait_ge(s_x1l, g)
                    for t in range(TILES):
                        u = a * TILES + t
                        for c in range(CHUNKS):
                            r = t * CHUNKS + c
                            if r in SUM_AT:
                                sum_products(g, a + 1, SUM_AT.index(r))
                            if c == PAIR_AT:
                                if t == 2:
                                    pe.wait_ge(s_diag[a % 2], DIAG_LOADS * (PER_TRIP // 2 * i + a // 2 + 1))
                                pair_sums(TRIP_TILES * i + u - 2, (u - 2) % TRIP_TILES)
                            n = u * CHUNKS + c - R_FROM
                            if 0 <= n < R_CHUNKS:
                                layer2(i, slice(n * FIELDS // R_CHUNKS, (n + 1) * FIELDS // R_CHUNKS))
                            if u == 0:
                                pe.wait_ge(s_w1l, c + 1)
                            layer1(i, a, t, c)
            pair_sums(TRIPS * TRIP_TILES - 2, TRIP_TILES - 2)
            pair_sums(TRIPS * TRIP_TILES - 1, TRIP_TILES - 1)
            layer2(TRIPS, slice(0, FIELDS))

        @block.scalar
        def _(act):
            def round_z(g, odd, t, z=z[:, :]):
                par = (odd + t) % 2
                act.wait_ge(s_z, GROUPS * g + t + 1)
                if not isinstance(g, int) or t > 1:
                    act.wait_ge(s_sum0, GROUPS * g + t - 1)
                rows = slice(0, P if t < FULL else LAST_ROWS)
                act.activation(z_h[par][rows, :], z[rows, :], ACT.Copy).then_inc(s_zh, 1)

            def round_x1(g, par):
                act.wait_ge(s_sum0, GROUPS * g + GROUPS)
                act.activation(x1_h[par][:, :], x1_ps[:, :], ACT.Identity, bias=b0_s[:, 0:1]).then_inc(s_x1h, 1)

            def weigh(i, a, t, c):
                q = (a * TILES + t) * CHUNKS + c
                bank = q % BANKS
                tile = TRIP_TILES * i + a * TILES + t
                k = ACT_CHUNKS.index(c)
                if k == 0:
                    act.wait_ge(s_x2, tile + 1)
                    dst = acc_a[t % 2]
                else:
                    act.wait_ge(s_chain, CHAIN * tile + k)
                    dst = prod[k - 1]
                act.wait_ge(s_y[bank], filled(i, q))
                for s in range(CJ):
                    last = act.activation(dst[:, s, :], y[bank][:, s, :], ACT.Copy,
                                          scale=xn[a % 2][:, t, CJ * c + s:CJ * c + s + 1])
                last.then_inc(s_act, 1)

            def round_x2(tile, par):
                act.wait_ge(s_x2, tile + 3)
                act.activation(x2_h[par][:, :], x2[par][:, :], ACT.Copy).then_inc(s_x2h, 1)

            def round_xn(g, par, loads):
                act.wait_ge(s_xn[par], loads)
                act.activation(xn_h[par][:, :, :], xn[par][:, :, :], ACT.Copy).then_inc(s_xnh, 1)

            def save_pair(tile, u):
                act.wait_ge(s_pair, tile + 3)
                act.activation(pair[:, :, TILE_B * u:TILE_B * u + TILE_B],
                               pair_ps[:, :, :].rearrange("k b j -> k j b"), ACT.Copy).then_inc(s_pair_sb, 1)

            def round_w1(q):
                act.wait_ge(s_w1[q], 16)
                act.activation(w1_h[:, fields_of(q), :], w1_f[:, fields_of(q), :], ACT.Copy).then_inc(s_w1h, 1)

            act.wait_ge(s_w0, 1)
            act.activation(w0_h[:, :, :], w0_a[:, :, :], ACT.Copy).then_inc(s_w0h, 1)
            act.activation(prod[-1][:, 0, 0:2], w0_a[:, 0, 0:2], ACT.Copy).then_inc(s_act, NA)
            act.activation(prod[-1][:, 1, 0:2], w0_a[:, 0, 0:2], ACT.Copy).then_inc(s_pair_sb, 1)
            for t in range(GROUPS):
                round_z(0, 0, t, z_first[t % 2])
                if t == 0:
                    act.wait_ge(s_w0l, 1)
                    for rows in (slice(0, NL), slice(LOW_ROW, LOW_ROW + NL)):
                        act.activation(w0_l[rows, FULL, :], w0_a[rows, FULL, :], ACT.Copy).then_inc(s_w0h, 1)
                if t >= FIRST_TILES:
                    round_w1(t - FIRST_TILES)
            act.wait_ge(s_consts, 3 * 16)
            round_x1(0, 0)
            round_xn(0, 0, 16)
            for q in range(GROUPS - FIRST_TILES, CHUNKS):
                round_w1(q)
            with act.Fori(0, TRIPS) as i:
                for a in range(PER_TRIP):
                    g = PER_TRIP * i + a + 1
                    act.wait_ge(s_xn[a % 2], 16 * (PER_TRIP // 2 * i + a // 2) + 16)
                    for t in range(TILES):
                        u = a * TILES + t
                        for c in ACT_CHUNKS:
                            r = t * CHUNKS + c
                            for k in range(GROUPS):
                                if r == own_chunk(ACT_CHUNKS, ROUND_AT[k]):
                                    round_z(g, a + 1, k)
                            if r == own_chunk(ACT_CHUNKS, X1_AT):
                                round_x1(g, (a + 1) % 2)
                            if c == SPLIT_AT:
                                round_x2(TRIP_TILES * i + u - 1, (u - 1) % 2)
                            if (t, c) == (2, 0):
                                round_xn(g, (a + 1) % 2, 16 * (PER_TRIP // 2 * i + (a + 1) // 2 + 1))
                            if c == SAVE_AT:
                                if u == 0:
                                    act.wait_ge(s_w1l, CHUNKS)
                                    act.wait_ge(s_ones, 1)
                                if u == 2:
                                    act.wait_ge(s_out1, i + 1)
                                save_pair(TRIP_TILES * i + u - 2, (u - 2) % TRIP_TILES)
                            weigh(i, a, t, c)
            round_x2(TRIPS * TRIP_TILES - 1, 1)
            save_pair(TRIPS * TRIP_TILES - 2, TRIP_TILES - 2)
            save_pair(TRIPS * TRIP_TILES - 1, TRIP_TILES - 1)

        @block.vector
        def _(dve):
            def form_z(g, par, t, z=z[:, :]):
                if t < FULL:
                    step = dve.tensor_tensor(z, xs[par][:, t, :], xr[par][:, :], ALU.mult)
                else:
                    step = dve.tensor_tensor(z[0:LAST_ROWS, :], xl[par][:, 0, :], xl[par][:, 1, :], ALU.mult)
                step.then_inc(s_z, 1)

            def low_z(g, odd, t, z=z[:, :]):
                par = (odd + t) % 2
                dve.wait_ge(s_zh, GROUPS * g + t + 1)
                if t < FULL:
                    rows, low = slice(0, P), z_l[par]
                else:
                    rows, low = slice(LOW_ROW, LOW_ROW + NL), z_h[par]
                dve.tensor_tensor(low[rows, :], z[rows, :], z_h[par][rows, :].bitcast(F32),
                                  ALU.subtract).then_inc(s_zl, 1)

            def low_x1(g, par):
                dve.wait_ge(s_x1h, g + 1)
                dve.scalar_tensor_tensor(out=x1_l[par][:, :], in0=x1_ps[:, :], scalar=b0_s[:, 0:1],
                                         in1=x1_h[par][:, :].bitcast(F32), op0=ALU.add,
                                         op1=ALU.subtract).then_inc(s_x1l, 1)

            def sum_out0(g):
                dve.tensor_reduce(out0[:, bass.ds(g * (STEP // EMB), STEP // EMB)],
                                  x1_ps[:, :].rearrange("h (b d) -> h b d", d=EMB), AX_X,
                                  ALU.add).then_inc(s_out0, 1)

            def low_xn(par):
                dve.tensor_tensor(xn_l[par][:, :, :], xn[par][:, :, :], xn_h[par][:, :, :].bitcast(F32),
                                  ALU.subtract).then_inc(s_xnl, 1)

            def weigh(i, a, t, c):
                q = (a * TILES + t) * CHUNKS + c
                bank = q % BANKS
                tile = TRIP_TILES * i + a * TILES + t
                done = dve_through(tile - 1, DVE_CHUNKS[-1])
                for s in range(fields_of(c).stop - fields_of(c).start):
                    x = xn[a % 2][:, t, CJ * c + s:CJ * c + s + 1]
                    f = CJ * DVE_CHUNKS.index(c) + s
                    acc = acc_d[t % 2][:, f % 2, :]
                    if f == 0:
                        dve.wait_ge(s_x2, tile + 1)
                    if s == 0:
                        dve.wait_ge(s_y[bank], filled(i, q))
                    if f > 1:
                        dve.wait_ge(s_dve, done + f - 1)
                    if f == 1:
                        step = dve.tensor_scalar(acc, y[bank][:, s, :], x, None, ALU.mult)
                    else:
                        step = dve.scalar_tensor_tensor(out=acc, in0=y[bank][:, s, :], scalar=x,
                                                        in1=acc if f else b1_row[:, :],
                                                        op0=ALU.mult, op1=ALU.add)
                    step.then_inc(s_dve, 1)

            def save_out1(i):
                dve.wait_ge(s_pair_sb, TRIP_TILES * i + 3)
                dve.tensor_scalar(out1[:, bass.ds(i * TRIP_B, TRIP_B)], pair[:, FIELDS, :], 1.0, None,
                                  ALU.mult).then_inc(s_out1, 1)

            def save_out2(i):
                dve.wait_ge(s_r, i + 1)
                dve.tensor_scalar(out2[:, bass.ds(i * TRIP_B, TRIP_B)], r_ps[:, :], b2_16[:, 0:1], None,
                                  ALU.add).then_inc(s_out2, 1)

            dve.memset(pair[:, FIELDS, :], 0.0).then_inc(s_ones, 1)
            dve.wait_ge(s_w0_in, 2 * 16)
            dve.tensor_tensor(w0_a[:, :, :], w0_a[:, :, :], w0_b[:, :, :], ALU.add).then_inc(s_w0, 1)
            dve.wait_ge(s_w0h, 1)
            dve.tensor_tensor(w0_l[:, :, :], w0_a[:, :, :], w0_h[:, :, :].bitcast(F32),
                              ALU.subtract).then_inc(s_w0l, 1)
            dve.wait_ge(s_first[0], 16 * (COPIES + 2))
            form_z(0, 0, 0, z_first[0])
            for t in range(GROUPS):
                if t + 1 < GROUPS:
                    if t + 1 == FIRST_TILES:
                        dve.wait_ge(s_first[1], 16 * (COPIES + 2))
                    if t > 0:
                        dve.wait_ge(s_zl, t)
                    form_z(0, 0, t + 1, z_first[(t + 1) % 2])
                if t > 1:
                    dve.wait_ge(s_sum0, t - 1)
                low_z(0, 0, t, z_first[t % 2])
            dve.wait_ge(s_consts, 3 * 16)
            dve.tensor_scalar(b0_16[:, :], b0_s[:, :], float(EMB), None, ALU.mult).then_inc(s_out0, 1)
            dve.tensor_scalar(b2_16[:, :], b2_s[:, :], float(EMB), None, ALU.mult).then_inc(s_out2, 1)
            low_x1(0, 0)
            dve.wait_ge(s_xnh, 1)
            low_xn(0)
            sum_out0(0)
            dve.memset(acc_d[1][:, 0, 0:2], 0.0).then_inc(s_dve, ND)
            dve.wait_ge(s_out2, 1)
            with dve.Fori(0, TRIPS) as i:
                for a in range(PER_TRIP):
                    g, par = PER_TRIP * i + a + 1, (a + 1) % 2
                    dve.wait_ge(s_xn[a % 2], 16 * (PER_TRIP // 2 * i + a // 2) + 16)
                    for t in range(TILES):
                        u = a * TILES + t
                        for c in DVE_CHUNKS:
                            r = t * CHUNKS + c
                            for k in range(GROUPS):
                                if r == own_chunk(DVE_CHUNKS, LOW_AT[k]):
                                    low_z(g, a + 1, k)
                            for k in range(GROUPS):
                                if r == own_chunk(DVE_CHUNKS, FORM_AT[k]):
                                    if k == 0:
                                        dve.wait_ge(s_x[par], X_LOADS * (PER_TRIP // 2 * i + a // 2 + 1))
                                    dve.wait_ge(s_zl, GROUPS * g + k)
                                    form_z(g, par, k)
                            if r == own_chunk(DVE_CHUNKS, X1_AT + 1):
                                low_x1(g, par)
                            if r == own_chunk(DVE_CHUNKS, OUT0_AT):
                                sum_out0(g)
                            if (t, c) == (2, 3):
                                dve.wait_ge(s_xnh, g + 1)
                                low_xn(par)
                            if (u, c) == (1, 7):
                                save_out1(i)
                            if (u, c) == (2, 3):
                                save_out2(i)
                            weigh(i, a, t, c)
            dve.wait_ge(s_out0, NSTEPS + 2)
            dve.tensor_scalar(out0[:, 0:BATCH], out0[:, 0:BATCH], b0_16[:, 0:1], None, ALU.add).then_inc(s_last, 1)
            save_out1(TRIPS)
            save_out2(TRIPS)

        @block.gpsimd
        def _(pool):
            def add(out_, in0, in1, done):
                pool.wait_ge(s_chain, done)
                return pool.tensor_tensor(out_, in0, in1, ALU.add)

            def low_x2(tile, par):
                pool.wait_ge(s_x2h, tile + 2)
                pool.tensor_tensor(x2_l[par][:, :], x2[par][:, :], x2_h[par][:, :].bitcast(F32),
                                   ALU.subtract).then_inc(s_x2l, 1)

            for diag in diag_h + diag_l:
                pool.memset(diag[:, :, :, :].bitcast(F32), 0.0).then_inc(s_clear, 1)
            pool.memset(x2[1][:, :], 0.0).then_inc(s_x2, 2)
            pool.memset(x2_h[0][:, :].bitcast(F32), 0.0).then_inc(s_clear, 1)
            pool.memset(x2_l[0][:, :].bitcast(F32), 0.0).then_inc(s_x2l, 1)
            pool.memset(acc_a[1][:, 0, 0:2], 0.0).then_inc(s_chain, CHAIN)
            for q in range(CHUNKS):
                pool.wait_ge(s_w1h, q + 1)
                pool.tensor_tensor(w1_l[:, fields_of(q), :], w1_f[:, fields_of(q), :],
                                   w1_h[:, fields_of(q), :].bitcast(F32), ALU.subtract).then_inc(s_w1l, 1)
            with pool.Fori(0, TRIPS) as i:
                for u in range(TRIP_TILES):
                    tile, par = TRIP_TILES * i + u, u % 2
                    whole, half = acc_a[par][:, :, :], acc_a[par][:, 0:2, :]
                    chained = CHAIN * (tile + 1)
                    for k in range(NA - 1):
                        pool.wait_ge(s_act, act_through(tile, ACT_CHUNKS[k + 1]))
                        add(whole, whole, prod[k][:, :, :], chained + k).then_inc(s_chain, 1)
                        if k == LOW_AFTER:
                            low_x2(tile - 1, 1 - par)
                    add(half, half, acc_a[par][:, 2:4, :], chained + NA - 1).then_inc(s_chain, 1)
                    pool.wait_ge(s_dve, dve_through(tile, DVE_CHUNKS[-1]))
                    add(half, half, acc_d[par][:, :, :], chained + NA).then_inc(s_chain, 1)
                    add(x2[par][:, :], acc_a[par][:, 0, :], acc_a[par][:, 1, :],
                        chained + CHAIN).then_inc(s_x2, 1)

            low_x2(TRIPS * TRIP_TILES - 1, 1)


def kernel(r_embedded_features, L0_rec_W0, L0_rec_b0, L0_rec_W1, L0_rec_b1, L0_rec_W2, L0_rec_b2):
    import concourse.bacc as bacc
    from concourse.bass_utils import run_bass_kernel_spmd

    x = np.asarray(r_embedded_features)
    f32 = x.dtype
    padded = COLS + 2 * STEP
    columns = np.zeros((FIELDS, padded), f32)
    columns[:, :COLS] = x.transpose(1, 0, 2).reshape(FIELDS, COLS)
    x_twice = np.concatenate([columns, columns])
    x_rep = np.concatenate([columns] * COPIES + [columns[:EXTRA]])
    x_last = np.stack([columns[[k for k, _ in LAST_PAIRS]], columns[[j for _, j in LAST_PAIRS]]], axis=1)
    x_row = np.zeros((NSTEPS + 1, P, TILES, JX), f32)
    x_row[:NSTEPS, :, :, :FIELDS] = x.transpose(0, 2, 1).reshape(NSTEPS, TILES, P, FIELDS).transpose(0, 2, 1, 3)
    x_row[:, :, :, FIELDS] = 1.0

    w0 = np.asarray(L0_rec_W0).reshape(HID, FIELDS, FIELDS)
    w0a = np.zeros((P, GROUPS, HID), f32)
    w0b = np.zeros((P, GROUPS, HID), f32)
    for t, pairs in enumerate(FULL_PAIRS + [LAST_PAIRS]):
        for row, pair in enumerate(pairs):
            if pair is not None:
                k, j = pair
                w0a[row, t] = w0[:, k, j]
                if j != k:
                    w0b[row, t] = w0[:, j, k]

    def by_k(w):
        return w.reshape(HID, FIELDS, HID).transpose(2, 1, 0).reshape(HID, FIELDS * HID)

    given = {
        "x_twice": x_twice, "x_rep": x_rep, "x_last": x_last, "x_row": x_row.reshape((NSTEPS + 1) * P, TILES, JX),
        "w0a": w0a.reshape(P, -1), "w0b": w0b.reshape(P, -1),
        "w1": by_k(np.asarray(L0_rec_W1)), "w2": by_k(np.asarray(L0_rec_W2)),
        "b0": np.asarray(L0_rec_b0), "b1": np.asarray(L0_rec_b1), "b2": np.asarray(L0_rec_b2),
    }
    given = {name: np.ascontiguousarray(a) for name, a in given.items()}
    nc = bacc.Bacc("TRN2", target_bir_lowering=False, num_devices=1)
    aps = [nc.dram_tensor(name, a.shape, mybir.dt.from_np(a.dtype), kind="ExternalInput").ap()
           for name, a in given.items()]
    out = nc.dram_tensor("out", (3, HID, BATCH), F32, kind="ExternalOutput").ap()
    cin_kernel(nc, *aps, out)
    got = run_bass_kernel_spmd(nc, [given], core_ids=[0]).results[0]["out"]
    return got.transpose(2, 0, 1).reshape(BATCH, 3 * HID)
```
